# Optimizing a Trainium2 kernel written in Bass

```python
import numpy as np
import jax
import jax.numpy as jnp

def _softmax(x, axis=-1):
    return jax.nn.softmax(x, axis=axis)

def _gelu(x):
    return jax.nn.gelu(x, approximate=True)

def _silu(x):
    return jax.nn.silu(x)

def _sigmoid(x):
    return jax.nn.sigmoid(x)

def _layernorm(x, axis=-1, eps=1e-05):
    m = jnp.mean(x, axis=axis, keepdims=True)
    v = jnp.var(x, axis=axis, keepdims=True)
    return (x - m) / jnp.sqrt(v + eps)

def _scatter_add(tgt, idx, src, axis=0):
    return tgt.at[idx].add(src)

def _segment_sum(src, seg, n):
    return jax.ops.segment_sum(src, seg, n)
kernel_name = 'mk_cond_seq_d1_seqx_r4_b30a02'

def setup_inputs(seed: int=0):
    np.random.seed(seed)
    _w = jnp.asarray

    def _rec_inputs():
        import jax
        import jax.numpy as jnp
        _rk = jax.random.key(seed)
        x = 7.22e-05 + 1 * jax.random.normal(jax.random.fold_in(_rk, 1), (2, 1024, 256), jnp.float32)
        _lenS = 1024 - jax.random.randint(jax.random.fold_in(_rk, 7), (2,), 0, max(1, 1024 // 4) + 1, jnp.int32)
        _lenS2 = 1024 - jax.random.randint(jax.random.fold_in(_rk, 8), (2,), 0, max(1, 1024 // 4) + 1, jnp.int32)
        cond_1024 = 0.0061147 + 1.02565 * jax.random.normal(jax.random.fold_in(_rk, 11), (2, 256), jnp.float32)
        return (x, cond_1024)
    x, cond_1024 = _rec_inputs()

    def _L0_cond_setup():
        import jax, jax.numpy as jnp
        import numpy as np
        DIM = 256
        MLP_RATIO = 4
        EPS = 1e-06

        def rmsnorm(x, w):
            return x * jax.lax.rsqrt(jnp.mean(x * x, axis=-1, keepdims=True) + EPS) * w

        def film(x, cond, w, b):
            ss = cond @ w + b
            scale, shift = jnp.split(ss, 2, axis=-1)
            return x * (1.0 + scale[:, None, :]) + shift[:, None, :]
        key = jax.random.key(seed)
        ks = jax.random.split(key, 16)
        B, N, D = (4, 512, DIM)
        H = D * MLP_RATIO
        s = lambda fan_in: 1.0 / np.sqrt(fan_in)
        return {'x': jax.random.normal(ks[0], (B, N, D), jnp.float32), 'cond': jax.random.normal(ks[1], (B, D), jnp.float32), 'norm1_w': jnp.ones((D,), jnp.float32), 'film1_w': jax.random.normal(ks[2], (D, 2 * D), jnp.float32) * s(D), 'film1_b': jnp.zeros((2 * D,), jnp.float32), 'q_w': jax.random.normal(ks[3], (D, D), jnp.float32) * s(D), 'q_b': jnp.zeros((D,), jnp.float32), 'k_w': jax.random.normal(ks[4], (D, D), jnp.float32) * s(D), 'k_b': jnp.zeros((D,), jnp.float32), 'v_w': jax.random.normal(ks[5], (D, D), jnp.float32) * s(D), 'v_b': jnp.zeros((D,), jnp.float32), 'proj_w': jax.random.normal(ks[6], (D, D), jnp.float32) * s(D), 'proj_b': jnp.zeros((D,), jnp.float32), 'norm2_w': jnp.ones((D,), jnp.float32), 'film2_w': jax.random.normal(ks[7], (D, 2 * D), jnp.float32) * s(D), 'film2_b': jnp.zeros((2 * D,), jnp.float32), 'mlp_w1': jax.random.normal(ks[8], (D, H), jnp.float32) * s(D), 'mlp_b1': jnp.zeros((H,), jnp.float32), 'mlp_w2': jax.random.normal(ks[9], (H, D), jnp.float32) * s(H), 'mlp_b2': jnp.zeros((D,), jnp.float32)}
    _L0_cond_all = _L0_cond_setup()
    _L0_cond_in = {k: v for k, v in _L0_cond_all.items() if k in ('norm1_w', 'film1_w', 'film1_b', 'q_w', 'q_b', 'k_w', 'k_b', 'v_w', 'v_b', 'proj_w', 'proj_b', 'norm2_w', 'film2_w', 'film2_b', 'mlp_w1', 'mlp_b1', 'mlp_w2', 'mlp_b2')}
    del _L0_cond_all
    return {'x': x, 'cond_1024': cond_1024, 'L0_cond_norm1_w': _L0_cond_in['norm1_w'], 'L0_cond_film1_w': _L0_cond_in['film1_w'], 'L0_cond_film1_b': _L0_cond_in['film1_b'], 'L0_cond_q_w': _L0_cond_in['q_w'], 'L0_cond_q_b': _L0_cond_in['q_b'], 'L0_cond_k_w': _L0_cond_in['k_w'], 'L0_cond_k_b': _L0_cond_in['k_b'], 'L0_cond_v_w': _L0_cond_in['v_w'], 'L0_cond_v_b': _L0_cond_in['v_b'], 'L0_cond_proj_w': _L0_cond_in['proj_w'], 'L0_cond_proj_b': _L0_cond_in['proj_b'], 'L0_cond_norm2_w': _L0_cond_in['norm2_w'], 'L0_cond_film2_w': _L0_cond_in['film2_w'], 'L0_cond_film2_b': _L0_cond_in['film2_b'], 'L0_cond_mlp_w1': _L0_cond_in['mlp_w1'], 'L0_cond_mlp_b1': _L0_cond_in['mlp_b1'], 'L0_cond_mlp_w2': _L0_cond_in['mlp_w2'], 'L0_cond_mlp_b2': _L0_cond_in['mlp_b2']}

def reference(x, cond_1024, L0_cond_norm1_w, L0_cond_film1_w, L0_cond_film1_b, L0_cond_q_w, L0_cond_q_b, L0_cond_k_w, L0_cond_k_b, L0_cond_v_w, L0_cond_v_b, L0_cond_proj_w, L0_cond_proj_b, L0_cond_norm2_w, L0_cond_film2_w, L0_cond_film2_b, L0_cond_mlp_w1, L0_cond_mlp_b1, L0_cond_mlp_w2, L0_cond_mlp_b2):
    import jax
    import jax.numpy as jnp

    def _L0_cond_ref(x, cond, norm1_w, film1_w, film1_b, q_w, q_b, k_w, k_b, v_w, v_b, proj_w, proj_b, norm2_w, film2_w, film2_b, mlp_w1, mlp_b1, mlp_w2, mlp_b2):
        import jax, jax.numpy as jnp
        import numpy as np
        DIM = 256
        MLP_RATIO = 4
        EPS = 1e-06

        def rmsnorm(x, w):
            return x * jax.lax.rsqrt(jnp.mean(x * x, axis=-1, keepdims=True) + EPS) * w

        def film(x, cond, w, b):
            ss = cond @ w + b
            scale, shift = jnp.split(ss, 2, axis=-1)
            return x * (1.0 + scale[:, None, :]) + shift[:, None, :]
        B, N, D = x.shape
        x_in = x
        h = film(rmsnorm(x, norm1_w), cond, film1_w, film1_b)
        Q = h @ q_w + q_b
        K = h @ k_w + k_b
        V = h @ v_w + v_b
        scores = jnp.einsum('bnd,bmd->bnm', Q, K) * D ** (-0.5)
        attn = jax.nn.softmax(scores, axis=-1)
        out = jnp.einsum('bnm,bmd->bnd', attn, V)
        x = x_in + (out @ proj_w + proj_b)
        x_in = x
        h = film(rmsnorm(x, norm2_w), cond, film2_w, film2_b)
        h = jax.nn.gelu(h @ mlp_w1 + mlp_b1, approximate=False) @ mlp_w2 + mlp_b2
        return x_in + h
    x = _L0_cond_ref(x, cond_1024, L0_cond_norm1_w, L0_cond_film1_w, L0_cond_film1_b, L0_cond_q_w, L0_cond_q_b, L0_cond_k_w, L0_cond_k_b, L0_cond_v_w, L0_cond_v_b, L0_cond_proj_w, L0_cond_proj_b, L0_cond_norm2_w, L0_cond_film2_w, L0_cond_film2_b, L0_cond_mlp_w1, L0_cond_mlp_b1, L0_cond_mlp_w2, L0_cond_mlp_b2)
    return x

_drawn_inputs = setup_inputs


def setup_inputs(seed=0):
    import zlib

    import numpy as np

    out = dict(_drawn_inputs(seed))
    spreads = {'L0_cond_norm1_w': (1.0, 0.2),
     'L0_cond_film1_b': (0.0, 0.1),
     'L0_cond_q_b': (0.0, 0.1),
     'L0_cond_k_b': (0.0, 0.1),
     'L0_cond_v_b': (0.0, 0.1),
     'L0_cond_proj_b': (0.0, 0.1),
     'L0_cond_norm2_w': (1.0, 0.2),
     'L0_cond_film2_b': (0.0, 0.1),
     'L0_cond_mlp_b1': (0.0, 0.1),
     'L0_cond_mlp_b2': (0.0, 0.1)}
    factors = {}
    for name, (base, spread) in spreads.items():
        noise = np.random.default_rng([zlib.crc32(name.encode()), seed]).standard_normal(out[name].shape)
        drawn = base * np.exp(spread * noise) if base else spread * noise
        out[name] = jnp.asarray(drawn.astype(out[name].dtype))
    for name, factor in factors.items():
        out[name] = (out[name] * factor).astype(out[name].dtype)
    return out
```

```python
from contextlib import ExitStack

import concourse.bass as bass
from concourse import mybir

F32 = mybir.dt.float32
F32R = mybir.dt.float32r
ALU = mybir.AluOpType
ACT = mybir.ActivationFunctionType
AX_X = mybir.AxisListType.X
ds = bass.ds

P = 128
HI, LO = 0, 1
PASSES = [(LO, HI), (HI, LO), (HI, HI)]
EPS = 1e-6


def film_block_kernel(nc, x, cond, norm1_w, film1_w, film1_b, q_w, q_b, k_w, k_b, v_w, v_b,
                      proj_w, proj_b, norm2_w, film2_w, film2_b, mlp_w1, mlp_b1, mlp_w2, mlp_b2, out):
    B, N, D = x.shape
    H = mlp_w1.shape[1]
    DT = D // P
    HT = H // P
    KT = N // P
    TILES = B * KT
    GT = 4
    GW = GT * P
    GROUPS = TILES // GT
    SCALE = float(D) ** -0.5
    VW = D + 2
    assert (B, D, GROUPS, TILES % 2, GW) == (2, 256, 4, 0, 512)

    NORM, FB, QB, KB, VB, B1, CND = (0, 12), (2, 14), 6, 8, 10, 18, 26
    NVEC = CND + B * DT
    FILM_BANK = (3, 6)

    ctx = ExitStack()
    with ctx:
        def sb(name, shape, dt=F32):
            return ctx.enter_context(nc.sbuf_tensor(name, shape, dt))

        def sem(name):
            return ctx.enter_context(nc.semaphore(name))

        psum = ctx.enter_context(nc.psum_tensor("psum", [P, 8, 512], F32))

        x_rows = sb("x_rows", [P, TILES, D])
        hT = sb("hT", [P, 2, DT, B * N], F32R)
        G_all = sb("G_all", [P, TILES, 2, DT, P], F32R)
        V_all = sb("V_all", [P, TILES, 2, D], F32R)
        w1 = sb("w1", [P, 2, DT, H], F32R)
        w2 = sb("w2", [P, 2, HT, D], F32R)
        raw = sb("raw", [P, 4096])
        probs = sb("probs", [P, 2, N])
        probsT = sb("probsT", [P, 2, 2, KT, P], F32R)
        g_tile = sb("g_tile", [P, 2, 2, DT, P], F32R)
        xn = sb("xn", [P, GT, D])
        h_full = sb("h_full", [P, DT, GW])
        ident = sb("ident", [P, P])
        ones_row = sb("ones_row", [1, P])
        vecs = sb("vecs", [32, P])
        vcol = sb("vcol", [P, 32])
        bias_rows = sb("bias_rows", [1, 2, D])
        add_row = sb("add_row", [P, 2, D])
        bq_wide = sb("bq_wide", [P, DT, P])
        bv_wide = sb("bv_wide", [P, DT, P])
        coef = sb("coef", [P, 2, 2 * DT, B])
        coef_tmp = sb("coef_tmp", [P, 2, DT, B])
        small = sb("small", [P, 8])
        sumsq = sb("sumsq", [P, 2 * TILES])
        meansq = sb("meansq", [P, 2 * TILES])
        rstd = sb("rstd", [P, 2 * TILES])
        power = sb("power", [P, GT])
        key_term = sb("key_term", [P, TILES])
        row_max = sb("row_max", [P, TILES])
        true_max = sb("true_max", [P, TILES])
        exp_bias = sb("exp_bias", [P, TILES])
        row_sum = sb("row_sum", [P, TILES])
        row_inv = sb("row_inv", [P, TILES])

        wq, wk, wv, wp = (raw[:, i * 512:(i + 1) * 512].rearrange("p (t n) -> p t n", t=DT) for i in range(4))
        film_w = [raw[:, 2048 + i * 1024:3072 + i * 1024].rearrange("p (t n) -> p t n", t=DT) for i in range(2)]
        w1_raw, w2_raw = raw[:, 0:2048], raw[:, 2048:4096]
        flat_probs = probs[:, :, :].rearrange("p a n -> p (a n)")
        wqT, wkT, wvT = (flat_probs[:, i * 512:(i + 1) * 512].rearrange("p (t n) -> p t n", t=DT) for i in range(3))
        gelu_full = flat_probs[:, 0:1024].rearrange("p (a n) -> p a n", a=2)
        gelu = G_all[:, :, :, :, :].rearrange("p t a d n -> p (t a d n)").rearrange(
            "p (m a n) -> p m a n", m=HT, a=2)
        flat_probsT = probsT[:, :, :, :, :].rearrange("p a s k n -> p (a s k n)")
        qk_w = flat_probsT[:, 0:2 * DT * D].rearrange("p (a t n) -> p a t n", a=2, t=DT)
        vp_w = flat_probsT[:, 2 * DT * D:2 * DT * (D + VW)].rearrange(
            "p (a t n) -> p a t n", a=2, t=DT)
        w1_flat = w1[:, :, :, :].rearrange("p a t n -> p a (t n)")
        w2_flat = w2[:, :, :, :].rearrange("p a t n -> p a (t n)")

        def bank(i, w=512):
            return psum[:, i, 0:w]

        vec_in, wqk_in, wvp_in, rows_in, mlp_in = map(sem, ("vec_in", "wqk_in", "wvp_in", "rows_in", "mlp_in"))
        film_in = [sem("film1_in"), sem("film2_in")]
        x_in = [sem(f"x_in{g}") for g in range(GROUPS)]
        g_in = [sem("g_in_even"), sem("g_in_odd")]
        stored = sem("stored")
        zeroed, ident_ready, ones_ready = sem("zeroed"), sem("ident_ready"), sem("ones_ready")
        turned = {k: sem(f"{k}_turned") for k in ("vec", "wq", "wk", "wv")}
        ready = {k: sem(f"{k}_ready") for k in ("vec", "wq", "wk", "wv")}
        film_done = [sem("film1_done"), sem("film2_done")]
        coef_tmp_ready, coef_ready = sem("coef_tmp_ready"), sem("coef_ready")
        qk_done, qk_hi, qk_ready = sem("qk_done"), sem("qk_hi"), sem("qk_ready")
        vp_done, vp_hi, vp_ready = sem("vp_done"), sem("vp_hi"), sem("vp_ready")
        bias_done, bias_ready = sem("bias_done"), sem("bias_ready")
        wide_ready, addrow_done, addrow_ready = sem("wide_ready"), sem("addrow_done"), sem("addrow_ready")
        mlp_hi, mlp_ready = sem("mlp_hi"), sem("mlp_ready")
        sq_done, mean_done, rstd_done, xn_done = map(sem, ("sq_done", "mean_done", "rstd_done", "xn_done"))
        xT_done, h_hi, h_ready = sem("xT_done"), sem("h_hi"), sem("h_ready")
        G_done, G_hi, G_ready = sem("G_done"), sem("G_hi"), sem("G_ready")
        V_done, V_hi, V_ready = sem("V_done"), sem("V_hi"), sem("V_ready")
        scores_done, max_done, true_max_done, exp_bias_ready = map(
            sem, ("scores_done", "max_done", "true_max_done", "exp_bias_ready"))
        exp_done, probs_turned, probsT_hi, probsT_ready = map(
            sem, ("exp_done", "probs_turned", "probsT_hi", "probsT_ready"))
        inv_done, attn_done, residual_ready, rows_done = map(
            sem, ("inv_done", "attn_done", "residual_ready", "rows_done"))
        hidden_done, gelu_done, gelu_ready, mlp_done = map(
            sem, ("hidden_done", "gelu_done", "gelu_ready", "mlp_done"))

        x_v = x.rearrange("b (p t) n -> p b t n", t=KT)
        out_v = out.rearrange("b (p t) n -> b t p n", t=KT)

        block = ctx.enter_context(nc.Block())

        @block.sync
        def _(sp):
            def load(dst, src, done):
                sp.dma_start(dst, src).then_inc(done, 16)

            def load_x(g):
                b, t = divmod(g * GT, KT)
                load(x_rows[:, g * GT:(g + 1) * GT, :], x_v[:, b, t:t + GT, :], x_in[g])

            def cut(w):
                return w.rearrange("(t p) n -> p t n", p=P)

            load(wq, cut(q_w), wqk_in)
            load(wk, cut(k_w), wqk_in)
            load_x(0)
            load(film_w[0], cut(film1_w), film_in[0])
            load(wv, cut(v_w), wvp_in)
            load(wp, cut(proj_w), wvp_in)
            load_x(1)
            load(film_w[1], cut(film2_w), film_in[1])
            load_x(2)
            load_x(3)
            sp.wait_ge(addrow_done, 1)
            load(w1_raw.rearrange("p (t n) -> p t n", t=DT), cut(mlp_w1), mlp_in)
            sp.wait_ge(film_done[1], 1)
            load(w2_raw.rearrange("p (t n) -> p t n", t=HT), cut(mlp_w2), mlp_in)

            def load_g(t, parity):
                sp.dma_start(g_tile[:, parity, :, :, :].bitcast(F32), G_all[:, ds(t, 1), :, :, :].bitcast(F32)
                             ).then_inc(g_in[parity], 16)

            sp.wait_ge(G_ready, DT)
            load_g(0, 0)
            load_g(1, 1)
            sp.wait_ge(G_ready, DT * GROUPS)
            with sp.Fori(0, TILES // 2 - 1) as i:
                for parity in range(2):
                    sp.wait_ge(scores_done, i * 2 + (parity + 1))
                    load_g(i * 2 + (2 + parity), parity)

            with sp.Fori(0, B) as b:
                for t in range(KT):
                    sp.wait_ge(rows_done, b * KT + (TILES + t + 1))
                    sp.dma_start(out_v[ds(b, 1), t, :, :].rearrange("b p n -> (b p) n"),
                                 x_rows[:, ds(b * KT + t, 1), :].rearrange("p t n -> p (t n)")
                                 ).then_inc(stored, 16)
            sp.wait_ge(stored, 16 * TILES)

        @block.gpsimd
        def _(pool):
            pool.memset(ident[:, :], 0.0).then_inc(zeroed, 1)
            pool.memset(ones_row[:, :], 1.0).then_inc(ones_ready, 1)
            pool.memset(power[:, :], -0.5).then_inc(ones_ready, 1)
            pool.wait_ge(zeroed, 1)
            pool.affine_select(out=ident[:, :], in_=ident[:, :], compare_op=ALU.not_equal, fill=1.0,
                               base=0, pattern=[[-1, P]], channel_multiplier=1).then_inc(ident_ready, 1)
            pool.wait_ge(ones_ready, 2)

            def inverse_rms(n):
                cols = ds(n * GT, GT)
                pool.wait_ge(sq_done, n + 1)
                pool.tensor_scalar(meansq[:, cols], sumsq[:, cols], 1.0 / D, EPS, ALU.mult, ALU.add
                                   ).then_inc(mean_done, 1)
                pool.wait_ge(mean_done, n + 1)
                pool.tensor_tensor(rstd[:, cols], meansq[:, cols], power[:, :], ALU.pow).then_inc(rstd_done, 1)

            for g in range(GROUPS):
                inverse_rms(g)

            pool.wait_ge(addrow_ready, 1)
            pool.wait_ge(xn_done, GROUPS)
            with pool.Fori(0, TILES) as t:
                row = x_rows[:, ds(t, 1), :].rearrange("p t n -> p (t n)")
                pool.tensor_tensor(row, row, add_row[:, 0, :], ALU.add).then_inc(residual_ready, 1)

            pool.wait_ge(mlp_in, 32)
            for src, dst in ((w1_raw, w1_flat), (w2_raw, w2_flat)):
                for c in range(0, 2048, 512):
                    s = slice(c, c + 512)
                    pool.tensor_scalar(dst[:, HI, s], src[:, s], 1.0, 0.0, ALU.mult, ALU.add).then_inc(mlp_hi, 1)
            for n, (src, dst) in enumerate(((w1_raw, w1_flat), (w2_raw, w2_flat))):
                pool.wait_ge(mlp_hi, 4 * (n + 1))
                for c in range(0, 2048, 512):
                    s = slice(c, c + 512)
                    pool.tensor_tensor(dst[:, LO, s], src[:, s], dst[:, HI, s].bitcast(F32), ALU.subtract
                                       ).then_inc(mlp_ready, 1)

            for g in range(GROUPS):
                inverse_rms(g + GROUPS)
                pool.wait_ge(xn_done, g + (GROUPS + 1))
                for j in range(GT):
                    row = x_rows[:, ds(g * GT + j, 1), :].rearrange("p t n -> p (t n)")
                    pool.tensor_tensor(row, row, add_row[:, 1, :], ALU.add).then_inc(residual_ready, 1)

        @block.scalar
        def _(act):
            places = [(NORM[0], norm1_w), (FB[0], film1_b), (QB, q_b), (KB, k_b), (VB, v_b), (NORM[1], norm2_w),
                      (FB[1], film2_b), (B1, mlp_b1)]
            for r, v in places:
                k = v.shape[0] // P
                act.dma_start(vecs[r:r + k, :], v.rearrange("(r n) -> r n", n=P)).then_inc(vec_in, 16)
            act.dma_start(vecs[CND:NVEC, :], cond.rearrange("b (r n) -> (b r) n", n=P)).then_inc(vec_in, 16)
            for i, v in enumerate((proj_b, mlp_b2)):
                act.dma_start(bias_rows[:, i, :], v.rearrange("(a n) -> a n", a=1)).then_inc(rows_in, 16)

            def squares(g):
                act.wait_ge(x_in[g], 16)
                for j in range(GT):
                    t = g * GT + j
                    last = act.activation(V_all[:, t, 0, :], x_rows[:, t, :], ACT.Square,
                                          accum_out=sumsq[:, t:t + 1])
                last.then_inc(sq_done, 1)

            def columns(n, which, b, tokens):
                act.wait_ge(xT_done, n + 1)
                for d in range(DT):
                    for dst in (h_full[:, d, :], hT[:, HI, d, tokens]):
                        act.activation(dst, bank(d), ACT.Identity, bias=coef[:, which, DT + d, b],
                                       scale=coef[:, which, d, b]).then_inc(h_hi, 1)

            squares(0)
            act.wait_ge(turned["vec"], 1)
            act.copy(vcol[:, 0:NVEC], bank(3, NVEC)).then_inc(ready["vec"], 1)
            act.wait_ge(turned["wq"], 1)
            act.copy(wqT.rearrange("p t n -> p (t n)"), bank(0)).then_inc(ready["wq"], 1)
            act.wait_ge(turned["wv"], 1)
            act.copy(wvT.rearrange("p t n -> p (t n)"), bank(2)).then_inc(ready["wv"], 1)
            act.wait_ge(qk_done, 1)
            act.copy(qk_w[:, HI, :, :].rearrange("p t n -> p (t n)"), bank(4)).then_inc(qk_hi, 1)
            act.wait_ge(bias_done, 1)
            act.copy(small[:, 0:3], bank(6, 3)).then_inc(bias_ready, 1)
            act.wait_ge(vp_done, 1)
            act.copy(vp_w[:, HI, :, 0:D], bank(5).rearrange("p (t n) -> p t n", t=DT)).then_inc(vp_hi, 1)
            for k in range(2):
                act.copy(vp_w[:, HI, :, D + k:D + k + 1], bank(6)[:, 3:5].rearrange("p (t n) -> p t n", t=DT)
                         ).then_inc(vp_hi, 1)
            act.wait_ge(addrow_done, 1)
            act.copy(add_row[:, :, :].rearrange("p a n -> p (a n)"), bank(7)).then_inc(addrow_ready, 1)

            def group_parts(g):
                for d in range(DT):
                    act.wait_ge(G_done, DT * g + d + 1)
                    act.activation(G_all[:, g * GT:(g + 1) * GT, HI, d, :],
                                   bank(2 + d).rearrange("p (t n) -> p t n", t=GT), ACT.Identity,
                                   bias=small[:, d:d + 1]).then_inc(G_hi, 1)
                for j in range(GT):
                    act.wait_ge(V_done, GT * g + j + 1)
                    act.copy(V_all[:, g * GT + j, HI, :], bank(4 + j, D)).then_inc(V_hi, 1)

            act.wait_ge(coef_ready, 1)
            for g in range(GROUPS):
                if g > 0:
                    act.wait_ge(h_ready, DT * g)
                columns(g, 0, slice(g // 2, g // 2 + 1), slice(g * GW, (g + 1) * GW))
                if g + 1 < GROUPS:
                    squares(g + 1)
                if g > 0:
                    group_parts(g - 1)
            group_parts(GROUPS - 1)

            def exp(t, parity):
                act.wait_ge(exp_bias_ready, t + 1)
                act.activation(probs[:, parity, :], psum[:, 2 * parity:2 * parity + 2, :].rearrange("p a n -> p (a n)"),
                               ACT.Exp, bias=exp_bias[:, ds(t, 1)], scale=SCALE,
                               accum_out=row_sum[:, ds(t, 1)]).then_inc(exp_done, 1)

            def turned_hi(t, parity):
                for half in range(2):
                    act.wait_ge(probs_turned, t * 2 + (half + 1))
                    act.copy(probsT[:, parity, HI, 4 * half:4 * half + 4, :].rearrange("p k n -> p (k n)"),
                             bank(4 + half)).then_inc(probsT_hi, 1)

            exp(0, 0)
            exp(1, 1)
            with act.Fori(0, TILES // 2 - 1) as i:
                for k in (1, 2):
                    turned_hi(i * 2 + (k - 1), (k - 1) % 2)
                    exp(i * 2 + (k + 1), (k + 1) % 2)
            turned_hi(TILES - 2, 0)

            def squares_after(g):
                act.wait_ge(rows_done, g * GT + GT)
                act.wait_ge(xT_done, g + GROUPS)
                for j in range(GT):
                    last = act.activation(xn[:, j, :], x_rows[:, ds(g * GT + j, 1), :].rearrange("p t n -> p (t n)"),
                                          ACT.Square, accum_out=sumsq[:, ds(g * GT + (TILES + j), 1)])
                last.then_inc(sq_done, 1)

            def columns_after(g):
                act.wait_ge(h_ready, g * DT + DT * GROUPS)
                columns(g + GROUPS, 1, ds(g // 2, 1), ds(g * GW, GW))

            squares_after(0)
            turned_hi(TILES - 1, 1)
            columns_after(0)

            def gelu_tile(g, m):
                n = g * HT + m
                act.wait_ge(hidden_done, n + 1)
                if m >= 2:
                    act.wait_ge(gelu_ready, n - 1)
                for dst in (gelu_full[:, m % 2, :], gelu[:, m, HI, :]):
                    act.activation(dst, bank(2 + m % 2), ACT.Gelu, bias=vcol[:, B1 + m:B1 + m + 1]
                                   ).then_inc(gelu_done, 1)

            def mlp(g, more):
                for m in range(HT):
                    gelu_tile(g, m)
                    if more and m == 1:
                        squares_after(g + 1)
                    if more and m == 5:
                        columns_after(g + 1)

            with act.Fori(0, GROUPS - 1) as g:
                mlp(g, True)
            mlp(GROUPS - 1, False)

        @block.vector
        def _(dve):
            dve.wait_ge(turned["wk"], 1)
            dve.tensor_copy(wkT.rearrange("p t n -> p (t n)"), bank(1)).then_inc(ready["wk"], 1)
            dve.wait_ge(ready["vec"], 1)
            dve.wait_ge(ident_ready, 1)
            for wide, r in ((bq_wide, QB), (bv_wide, VB)):
                for d in range(DT):
                    dve.tensor_scalar(wide[:, d, :], ident[:, :], 0.0, vcol[:, r + d:r + d + 1], ALU.mult, ALU.add
                                      ).then_inc(wide_ready, 1)

            def coefficients(f):
                dve.wait_ge(film_done[f], 1)
                sums = bank(FILM_BANK[f])
                for d in range(DT):
                    dve.tensor_scalar(coef_tmp[:, f, d, :], sums[:, B * d:B * d + B],
                                      vcol[:, FB[f] + d:FB[f] + d + 1], 1.0, ALU.add, ALU.add
                                      ).then_inc(coef_tmp_ready, 1)
                    k = DT + d
                    dve.tensor_scalar(coef[:, f, k, :], sums[:, B * k:B * k + B],
                                      vcol[:, FB[f] + k:FB[f] + k + 1], None, ALU.add)
                dve.wait_ge(coef_tmp_ready, DT * (f + 1))
                for d in range(DT):
                    last = dve.tensor_scalar(coef[:, f, d, :], coef_tmp[:, f, d, :],
                                             vcol[:, NORM[f] + d:NORM[f] + d + 1], None, ALU.mult)
                last.then_inc(coef_ready, 1)

            def normed_rows(n, t):
                dve.wait_ge(rstd_done, n + 1)
                for j in range(GT):
                    last = dve.tensor_scalar(xn[:, j, :], x_rows[:, ds(t + j, 1), :].rearrange("p t n -> p (t n)"),
                                             rstd[:, ds(n * GT + j, 1)], None, ALU.mult)
                last.then_inc(xn_done, 1)

            def low_columns(n, tokens):
                for d in range(DT):
                    dve.wait_ge(h_hi, n * (2 * DT) + (2 * d + 2))
                    dve.tensor_tensor(hT[:, LO, d, tokens], h_full[:, d, :], hT[:, HI, d, tokens].bitcast(F32),
                                      ALU.subtract).then_inc(h_ready, 1)

            coefficients(0)
            normed_rows(0, 0)
            dve.wait_ge(qk_hi, 1)
            dve.tensor_tensor(qk_w[:, LO, :, :].rearrange("p t n -> p (t n)"), bank(4),
                              qk_w[:, HI, :, :].rearrange("p t n -> p (t n)").bitcast(F32), ALU.subtract
                              ).then_inc(qk_ready, 1)
            dve.wait_ge(vp_hi, 3)
            dve.tensor_tensor(vp_w[:, LO, :, 0:D], bank(5).rearrange("p (t n) -> p t n", t=DT),
                              vp_w[:, HI, :, 0:D].bitcast(F32), ALU.subtract).then_inc(vp_ready, 1)
            for k in range(2):
                dve.tensor_tensor(vp_w[:, LO, :, D + k:D + k + 1], bank(6)[:, 3:5].rearrange("p (t n) -> p t n", t=DT),
                                  vp_w[:, HI, :, D + k:D + k + 1].bitcast(F32), ALU.subtract).then_inc(vp_ready, 1)

            def group_parts(g):
                for d in range(DT):
                    dve.wait_ge(G_hi, DT * g + d + 1)
                    dve.scalar_tensor_tensor(out=G_all[:, g * GT:(g + 1) * GT, LO, d, :],
                                             in0=bank(2 + d).rearrange("p (t n) -> p t n", t=GT),
                                             scalar=small[:, d:d + 1],
                                             in1=G_all[:, g * GT:(g + 1) * GT, HI, d, :].bitcast(F32),
                                             op0=ALU.add, op1=ALU.subtract).then_inc(G_ready, 1)
                for j in range(GT):
                    t = g * GT + j
                    dve.wait_ge(V_hi, t + 1)
                    dve.tensor_scalar(key_term[:, t:t + 1], bank(4 + j)[:, D:D + 1], small[:, 2:3], None, ALU.add)
                    dve.tensor_tensor(V_all[:, t, LO, :], bank(4 + j, D), V_all[:, t, HI, :].bitcast(F32),
                                      ALU.subtract).then_inc(V_ready, 1)

            for g in range(GROUPS):
                low_columns(g, slice(g * GW, (g + 1) * GW))
                if g + 1 < GROUPS:
                    dve.wait_ge(xT_done, g + 1)
                    normed_rows(g + 1, (g + 1) * GT)
                if g == 0:
                    coefficients(1)
                if g > 0:
                    group_parts(g - 1)
            group_parts(GROUPS - 1)

            def row_maximum(t, parity):
                col = ds(t, 1)
                dve.wait_ge(scores_done, t + 1)
                dve.reduce_max(row_max[:, col], psum[:, 2 * parity:2 * parity + 2, :].rearrange("p a n -> p (a n)"),
                               AX_X).then_inc(max_done, 1)
                dve.wait_ge(max_done, t + 1)
                dve.tensor_tensor(true_max[:, col], row_max[:, col], key_term[:, col], ALU.add
                                  ).then_inc(true_max_done, 1)
                dve.wait_ge(true_max_done, t + 1)
                dve.tensor_scalar(exp_bias[:, col], true_max[:, col], key_term[:, col], -SCALE,
                                  ALU.subtract, ALU.mult).then_inc(exp_bias_ready, 1)

            def turned_lo(t, parity):
                for half in range(2):
                    dve.wait_ge(probsT_hi, t * 2 + (half + 1))
                    k = slice(4 * half, 4 * half + 4)
                    dve.tensor_tensor(probsT[:, parity, LO, k, :].rearrange("p k n -> p (k n)"), bank(4 + half),
                                      probsT[:, parity, HI, k, :].rearrange("p k n -> p (k n)").bitcast(F32),
                                      ALU.subtract).then_inc(probsT_ready, 1)

            def add_attention(t, parity):
                col = ds(t, 1)
                dve.wait_ge(attn_done, t + 1)
                dve.reciprocal(row_inv[:, col], row_sum[:, col]).then_inc(inv_done, 1)
                dve.wait_ge(inv_done, t + 1)
                dve.wait_ge(residual_ready, t + 1)
                row = x_rows[:, col, :].rearrange("p t n -> p (t n)")
                dve.scalar_tensor_tensor(out=row, in0=bank(6 + parity, D), scalar=row_inv[:, col], in1=row,
                                         op0=ALU.mult, op1=ALU.add).then_inc(rows_done, 1)

            row_maximum(0, 0)
            row_maximum(1, 1)
            with dve.Fori(0, TILES // 2 - 1) as i:
                for k in (1, 2):
                    turned_lo(i * 2 + (k - 1), (k - 1) % 2)
                    row_maximum(i * 2 + (k + 1), (k + 1) % 2)
                    add_attention(i * 2 + (k - 1), (k - 1) % 2)
            turned_lo(TILES - 2, 0)
            add_attention(TILES - 2, 0)
            normed_rows(GROUPS, 0)
            turned_lo(TILES - 1, 1)
            add_attention(TILES - 1, 1)
            low_columns(GROUPS, slice(0, GW))

            def gelu_low(g, m):
                n = g * HT + m
                dve.wait_ge(gelu_done, n * 2 + 2)
                dve.tensor_tensor(gelu[:, m, LO, :], gelu_full[:, m % 2, :], gelu[:, m, HI, :].bitcast(F32),
                                  ALU.subtract).then_inc(gelu_ready, 1)

            def mlp(g, more):
                for m in range(HT):
                    gelu_low(g, m)
                    if more and m == 2:
                        normed_rows(g + (GROUPS + 1), g * GT + GT)
                    if more and m == 6:
                        low_columns(g + (GROUPS + 1), ds(g * GW + GW, GW))
                dve.wait_ge(mlp_done, g + 1)
                for j in range(GT):
                    dve.wait_ge(residual_ready, g * GT + (TILES + j + 1))
                    row = x_rows[:, ds(g * GT + j, 1), :].rearrange("p t n -> p (t n)")
                    dve.tensor_tensor(row, bank(4 + j, D), row, ALU.add).then_inc(rows_done, 1)

            with dve.Fori(0, GROUPS - 1) as g:
                mlp(g, True)
            mlp(GROUPS - 1, False)

        @block.tensor
        def _(pe):
            def transpose_weight(w, to, what):
                for i in range(DT):
                    for e in range(DT):
                        last = pe.transpose(bank(to)[:, e * D + i * P:e * D + i * P + P], w[:, i, e * P:(e + 1) * P],
                                            ident[:, :])
                last.then_inc(turned[what], 1)

            def film(f):
                pe.wait_ge(film_in[f], 16)
                for k in range(2 * DT):
                    for d in range(DT):
                        last = pe.matmul(bank(FILM_BANK[f])[:, B * k:B * k + B], film_w[f][:, d, k * P:(k + 1) * P],
                                         vcol[:, CND + d:NVEC:DT], start=(d == 0), stop=(d == DT - 1))
                last.then_inc(film_done[f], 1)

            pe.wait_ge(ident_ready, 1)
            pe.wait_ge(vec_in, 16 * 9)
            pe.transpose(bank(3, NVEC), vecs[0:NVEC, :], ident[0:NVEC, 0:NVEC]).then_inc(turned["vec"], 1)
            pe.wait_ge(wqk_in, 32)
            transpose_weight(wq, 0, "wq")
            transpose_weight(wk, 1, "wk")
            pe.wait_ge(ready["vec"], 1)
            film(0)
            pe.wait_ge(wvp_in, 32)
            transpose_weight(wv, 2, "wv")
            pe.wait_ge(ready["wq"], 1)
            pe.wait_ge(ready["wk"], 1)
            for i in range(DT):
                for e in range(DT):
                    last = pe.matmul(bank(4)[:, i * D:(i + 1) * D], wqT[:, e, i * P:(i + 1) * P], wkT[:, e, :],
                                     start=(e == 0), stop=(e == DT - 1))
            last.then_inc(qk_done, 1)
            pe.wait_ge(wide_ready, 2 * DT)

            def columns_of(col, w, rhs, start=0):
                for e in range(DT):
                    last = pe.matmul(bank(6)[:, col:col + 1], w(e), rhs(e), start=(e == 0), stop=(e == DT - 1))
                return last

            for j in range(DT):
                columns_of(j, lambda e: wkT[:, e, j * P:(j + 1) * P], lambda e: vcol[:, QB + e:QB + e + 1])
            columns_of(2, lambda e: bq_wide[:, e, :], lambda e: vcol[:, KB + e:KB + e + 1])
            for i in range(DT):
                last = columns_of(3 + i, lambda e: wqT[:, e, i * P:(i + 1) * P], lambda e: vcol[:, KB + e:KB + e + 1])
            last.then_inc(bias_done, 1)
            pe.wait_ge(ready["wv"], 1)
            for i in range(DT):
                for e in range(DT):
                    last = pe.matmul(bank(5)[:, i * D:(i + 1) * D], wvT[:, e, i * P:(i + 1) * P], wp[:, e, :],
                                     start=(e == 0), stop=(e == DT - 1))
            last.then_inc(vp_done, 1)
            pe.wait_ge(rows_in, 32)
            pe.wait_ge(ones_ready, 1)
            for e in range(DT):
                pe.matmul(bank(7)[:, 0:D], bv_wide[:, e, :], wp[:, e, :], start=(e == 0), stop=False)
            pe.matmul(bank(7)[:, 0:D], ones_row[:, :], bias_rows[:, 0, :], start=False, stop=True)
            pe.matmul(bank(7)[:, D:2 * D], ones_row[:, :], bias_rows[:, 1, :], start=True, stop=True
                      ).then_inc(addrow_done, 1)

            def transpose_rows(n):
                pe.wait_ge(xn_done, n + 1)
                for d in range(DT):
                    for j in range(GT):
                        last = pe.transpose(bank(d)[:, j * P:(j + 1) * P], xn[:, j, d * P:(d + 1) * P], ident[:, :])
                last.then_inc(xT_done, 1)

            def split_matmul(dst, stationary, moving, tiles):
                n = len(tiles) * len(PASSES)
                for a, b in PASSES:
                    for k in tiles:
                        n -= 1
                        last = pe.matmul(dst, stationary(a, k), moving(b, k),
                                         start=(n == len(tiles) * len(PASSES) - 1), stop=(n == 0))
                return last

            def project_g(g):
                pe.wait_ge(h_ready, DT * (g + 1))
                if g > 0:
                    pe.wait_ge(G_ready, DT * g)
                s = slice(g * GW, (g + 1) * GW)
                for j in range(DT):
                    split_matmul(bank(2 + j), lambda a, k: qk_w[:, a, k, j * P:(j + 1) * P],
                                 lambda b, k: hT[:, b, k, s], range(DT)).then_inc(G_done, 1)

            def project_v(g):
                for j in range(GT):
                    if g > 0:
                        pe.wait_ge(V_ready, GT * (g - 1) + j + 1)
                    t = g * GT + j
                    split_matmul(bank(4 + j, VW), lambda a, k: hT[:, a, k, t * P:(t + 1) * P],
                                 lambda b, k: vp_w[:, b, k, :], range(DT)).then_inc(V_done, 1)

            pe.wait_ge(ready["wk"], 1)
            transpose_rows(0)
            pe.wait_ge(qk_ready, 1)
            for g in range(GROUPS):
                if g + 1 < GROUPS:
                    pe.wait_ge(h_hi, 2 * DT * (g + 1))
                    transpose_rows(g + 1)
                project_g(g)
                if g == 0:
                    pe.wait_ge(vp_ready, 3)
                    film(1)
                    pe.wait_ge(addrow_ready, 1)
                    pe.wait_ge(coef_ready, 2)
                project_v(g)

            def scores(t, parity, b):
                for half in range(2):
                    last = split_matmul(bank(2 * parity + half), lambda a, k: g_tile[:, parity, a, k, :],
                                        lambda s, k: hT[:, s, k, ds(b * N + half * 512, 512)], range(DT))
                last.then_inc(scores_done, 1)

            def transpose_probs(t, parity):
                pe.wait_ge(exp_done, t + 1)
                for half in range(2):
                    for j in range(4):
                        k = 4 * half + j
                        last = pe.transpose(bank(4 + half)[:, j * P:(j + 1) * P], probs[:, parity, k * P:(k + 1) * P],
                                            ident[:, :])
                    last.then_inc(probs_turned, 1)

            def attention(t, parity, b):
                n = 0
                for half in range(2):
                    pe.wait_ge(probsT_ready, t * 2 + (half + 1))
                    for k in range(4 * half, 4 * half + 4):
                        for a, s in PASSES:
                            last = pe.matmul(bank(6 + parity, D), probsT[:, parity, a, k, :],
                                             V_all[:, ds(b * KT + k, 1), s, :].rearrange("p t n -> p (t n)"),
                                             start=(n == 0), stop=(n == KT * len(PASSES) - 1))
                            n += 1
                last.then_inc(attn_done, 1)

            pe.wait_ge(G_ready, DT * GROUPS)
            pe.wait_ge(g_in[0], 16)
            scores(0, 0, 0)
            pe.wait_ge(g_in[1], 16)
            scores(1, 1, 0)
            pe.wait_ge(V_ready, TILES)
            transpose_probs(0, 0)
            with pe.Fori(0, TILES // 2 - 1) as i:
                for k in (1, 2):
                    nxt, now = (k + 1) % 2, k % 2
                    pe.wait_ge(g_in[nxt], (i * 2 + (k + 1)) // 2 * 16 + 16)
                    scores(None, nxt, (i * 2 + (k + 1)) // KT)
                    attention(i * 2 + (k - 1), nxt, (i * 2 + (k - 1)) // KT)
                    transpose_probs(i * 2 + k, now)
            attention(TILES - 2, 0, 1)
            transpose_probs(TILES - 1, 1)
            transpose_rows(GROUPS)
            attention(TILES - 1, 1, 1)

            def hidden(g, m):
                n = g * HT + m
                if m >= 2:
                    pe.wait_ge(gelu_done, n * 2 - 2)
                split_matmul(bank(2 + m % 2), lambda a, k: w1[:, a, k, m * P:(m + 1) * P],
                             lambda b, k: hT[:, b, k, ds(g * GW, GW)], range(DT)).then_inc(hidden_done, 1)

            def project_hidden(g, m):
                pe.wait_ge(gelu_ready, g * HT + (m + 1))
                for j in range(GT):
                    for n, (a, b) in enumerate(PASSES):
                        last = pe.matmul(bank(4 + j, D), gelu[:, m, a, j * P:(j + 1) * P], w2[:, b, m, :],
                                         start=(m == 0 and n == 0), stop=(m == HT - 1 and n == len(PASSES) - 1))
                if m == HT - 1:
                    last.then_inc(mlp_done, 1)

            def mlp(g, more):
                pe.wait_ge(h_ready, g * DT + DT * (GROUPS + 1))
                for m in range(HT):
                    hidden(g, m)
                    if more and m == 4:
                        transpose_rows(g + (GROUPS + 1))
                    if m == 2:
                        pe.wait_ge(rows_done, g * GT + TILES)
                    if m >= 2:
                        project_hidden(g, m - 2)
                project_hidden(g, HT - 2)
                project_hidden(g, HT - 1)

            pe.wait_ge(mlp_ready, 8)
            with pe.Fori(0, GROUPS - 1) as g:
                mlp(g, True)
            mlp(GROUPS - 1, False)


_INS = ['x', 'cond_1024'] + ['L0_cond_' + n for n in (
    'norm1_w', 'film1_w', 'film1_b', 'q_w', 'q_b', 'k_w', 'k_b', 'v_w', 'v_b', 'proj_w', 'proj_b',
    'norm2_w', 'film2_w', 'film2_b', 'mlp_w1', 'mlp_b1', 'mlp_w2', 'mlp_b2')]


def kernel(**inputs):
    import numpy as _np
    import concourse.bacc as _bacc
    from concourse import mybir as _mybir
    from concourse.bass_utils import run_bass_kernel_spmd as _run

    nc = _bacc.Bacc("TRN2", target_bir_lowering=False, num_devices=1)
    arrays, args = {}, []
    for name in _INS:
        a = _np.ascontiguousarray(inputs[name])
        arrays[f"in_{name}_dram"] = a
        args.append(nc.dram_tensor(f"in_{name}_dram", a.shape, _mybir.dt.from_np(a.dtype), kind="ExternalInput").ap())
    shape = arrays["in_x_dram"].shape
    args.append(nc.dram_tensor("out_0_dram", shape, _mybir.dt.float32, kind="ExternalOutput").ap())
    film_block_kernel(nc, *args)
    r = _run(nc, [arrays], core_ids=[0])
    return r.results[0]["out_0_dram"]
```

```python
from contextlib import ExitStack

import concourse.bass as bass
from concourse import mybir

F32 = mybir.dt.float32
F32R = mybir.dt.float32r
ALU = mybir.AluOpType
ACT = mybir.ActivationFunctionType
AX_X = mybir.AxisListType.X
ds = bass.ds

P = 128
HI, LO = 0, 1
PASSES = [(LO, HI), (HI, LO), (HI, HI)]
EPS = 1e-6


NORM, FB, VB, B1 = (0, 8), (2, 10), 6, 14
NVEC = 22


def film_block_kernel(nc, x, vectors, rows, qk_weights, vp_weights, k_w, film1_wT, film2_wT, out_bias,
                      mlp_w1, mlp_w2, out):
    B, N, D = x.shape
    H = mlp_w1.shape[2]
    DT = D // P
    HT = H // P
    KT = N // P
    TILES = B * KT
    GT = 4
    GW = GT * P
    GROUPS = TILES // GT
    SCALE = float(D) ** -0.5
    LAST = TILES // 2 - 2
    VW = D + 2
    assert (B, D, GROUPS, TILES % 2, GW) == (2, 256, 4, 0, 512)

    KW = D + 2

    ctx = ExitStack()
    with ctx:
        def sb(name, shape, dt=F32):
            return ctx.enter_context(nc.sbuf_tensor(name, shape, dt))

        def sem(name):
            return ctx.enter_context(nc.semaphore(name))

        psum = ctx.enter_context(nc.psum_tensor("psum", [P, 8, 512], F32))

        x_rows = sb("x_rows", [P, TILES, D])
        hT = sb("hT", [P, 2, DT, B * N], F32R)
        G_all = sb("G_all", [P, TILES, 2, DT, P], F32R)
        V_all = sb("V_all", [P, TILES, 2, D], F32R)
        w1 = sb("w1", [P, 2, DT, H], F32R)
        w2 = sb("w2", [P, 2, HT, D], F32R)
        raw = sb("raw", [P, DT * (3 * D + KW + 4 * D)])
        probs = sb("probs", [P, 2, N])
        probsT = sb("probsT", [P, 2, 2, KT, P], F32R)
        g_tile = sb("g_tile", [P, 2, 2, DT, P], F32R)
        xn = sb("xn", [P, GT, D])
        h_full = sb("h_full", [P, DT, GW])
        ident = sb("ident", [P, P])
        vcol = sb("vcol", [P, NVEC])
        add_row = sb("add_row", [P, 2, D])
        coef = sb("coef", [P, 2, B, 2 * DT])
        film_sum = sb("film_sum", [P, 2, B, 2 * DT])
        small = sb("small", [P, 8])
        sumsq = sb("sumsq", [P, 2 * TILES])
        meansq = sb("meansq", [P, 2 * TILES])
        rstd = sb("rstd", [P, 2 * TILES])
        power = sb("power", [P, GT])
        key_term = sb("key_term", [P, TILES])
        row_max = sb("row_max", [P, TILES])
        true_max = sb("true_max", [P, TILES])
        exp_bias = sb("exp_bias", [P, TILES])
        row_sum = sb("row_sum", [P, TILES])
        row_inv = sb("row_inv", [P, TILES])

        at = [0]

        def weight(width):
            part = raw[:, at[0]:at[0] + DT * width]
            at[0] += DT * width
            return part.rearrange("p (t n) -> p t n", t=DT)

        qk_raw, wvT, wp = weight(D + KW), weight(D), weight(D)
        wqT, wkT = qk_raw[:, :, 0:D], qk_raw[:, :, D:]
        QK_END, VP_END = DT * (D + KW), at[0]
        film_wT = [weight(2 * D).rearrange("p t n -> p (t n)").rearrange("p (k d) -> p k d", d=D) for _ in range(2)]
        w1_raw, w2_raw = raw[:, 0:DT * H], raw[:, VP_END:VP_END + HT * D]
        flat_probs = probs[:, :, :].rearrange("p a n -> p (a n)")
        bv_wide = flat_probs[:, 0:DT * P].rearrange("p (t n) -> p t n", t=DT)
        wk = flat_probs[:, 256:256 + DT * D].rearrange("p (t n) -> p t n", t=DT)
        wide_rows = flat_probs[:, 768:768 + (B + 2) * D].rearrange("p (r n) -> p r n", n=D)
        gelu_full = flat_probs[:, 0:1024].rearrange("p (a n) -> p a n", a=2)
        gelu = G_all[:, :, :, :, :].rearrange("p t a d n -> p (t a d n)").rearrange(
            "p (m a n) -> p m a n", m=HT, a=2)
        flat_probsT = probsT[:, :, :, :, :].rearrange("p a s k n -> p (a s k n)")
        qk_w = flat_probsT[:, 0:2 * DT * D].rearrange("p (a t n) -> p a t n", a=2, t=DT)
        vp_w = flat_probsT[:, 2 * DT * D:2 * DT * (D + VW)].rearrange(
            "p (a t n) -> p a t n", a=2, t=DT)
        w1_flat = w1[:, :, :, :].rearrange("p a t n -> p a (t n)")
        w2_flat = w2[:, :, :, :].rearrange("p a t n -> p a (t n)")

        def bank(i, w=512):
            return psum[:, i, 0:w]

        vec_in, wvp_in, rows_in, mlp_in = map(sem, ("vec_in", "wvp_in", "rows_in", "mlp_in"))
        wqk_in = [sem(f"wqk_in{e}") for e in range(DT)]
        film_in = [sem("film1_in"), sem("film2_in")]
        x_in = [sem(f"x_in{g}") for g in range(GROUPS)]
        x_half_in = sem("x_half_in")
        g_in = [sem("g_in_even"), sem("g_in_odd")]
        stored = sem("stored")
        zeroed, ident_ready, ones_ready = sem("zeroed"), sem("ident_ready"), sem("ones_ready")
        k_in, wide_in, film_sums = sem("k_in"), sem("wide_in"), sem("film_sums")
        shift_ready, coef_ready = sem("shift_ready"), sem("coef_ready")
        qk_done, qk_hi, qk_ready = sem("qk_done"), sem("qk_hi"), sem("qk_ready")
        vp_done, vp_hi, vp_ready = sem("vp_done"), sem("vp_hi"), sem("vp_ready")
        bias_ready = sem("bias_ready")
        wide_ready, addrow_done, addrow_ready = sem("wide_ready"), sem("addrow_done"), sem("addrow_ready")
        mlp_hi, mlp_ready = sem("mlp_hi"), sem("mlp_ready")
        sq_done, mean_done, rstd_done, xn_done = map(sem, ("sq_done", "mean_done", "rstd_done", "xn_done"))
        dve_sq_done = sem("dve_sq_done")
        xT_done, h_done, h_hi, h_ready = sem("xT_done"), sem("h_done"), sem("h_hi"), sem("h_ready")
        G_done, G_hi, G_ready = sem("G_done"), sem("G_hi"), sem("G_ready")
        V_done, V_hi, V_ready = sem("V_done"), sem("V_hi"), sem("V_ready")
        scores_done, max_done, true_max_done, exp_bias_ready = map(
            sem, ("scores_done", "max_done", "true_max_done", "exp_bias_ready"))
        exp_done, probs_turned, probsT_hi, probsT_ready = map(
            sem, ("exp_done", "probs_turned", "probsT_hi", "probsT_ready"))
        inv_done, attn_done, residual_ready, rows_done = map(
            sem, ("inv_done", "attn_done", "residual_ready", "rows_done"))
        hidden_done, gelu_done, gelu_ready, mlp_done = map(
            sem, ("hidden_done", "gelu_done", "gelu_ready", "mlp_done"))

        x_v = x.rearrange("b (p t) n -> p b t n", t=KT)
        out_v = out.rearrange("b (p t) n -> p b t n", t=KT)

        block = ctx.enter_context(nc.Block())

        @block.sync
        def _(sp):
            def load(dst, src, done):
                sp.dma_start(dst, src).then_inc(done, 16)

            def load_x(g):
                b, t = divmod(g * GT, KT)
                load(x_rows[:, g * GT:(g + 1) * GT, :], x_v[:, b, t:t + GT, :], x_in[g])

            load(x_rows[:, 0:GT // 2, :], x_v[:, 0, 0:GT // 2, :], x_half_in)
            load(x_rows[:, GT // 2:GT, :], x_v[:, 0, GT // 2:GT, :], x_in[0])
            for e in range(DT):
                load(qk_raw[:, e, :], qk_weights[:, e, :], wqk_in[e])
            load(vcol[:, :], vectors, vec_in)
            load(wide_rows[:, 0:B, :], rows[0:B, :].partition_broadcast(P), wide_in)
            load(film_wT[0], film1_wT, film_in[0])
            load(raw[:, QK_END:VP_END], vp_weights, wvp_in)
            load_x(1)
            load(wk, k_w, k_in)
            load(wide_rows[:, B:B + 2, :], rows[B:B + 2, :].partition_broadcast(P), k_in)
            load(add_row[:, :, :], out_bias.partition_broadcast(P), rows_in)
            load_x(2)
            load_x(3)
            load(film_wT[1], film2_wT, film_in[1])
            sp.wait_ge(addrow_done, 1)
            load(w1_raw.rearrange("p (t n) -> p t n", t=DT), mlp_w1, mlp_in)

            def load_g(t, parity):
                sp.dma_start(g_tile[:, parity, :, :, :].bitcast(F32), G_all[:, ds(t, 1), :, :, :].bitcast(F32)
                             ).then_inc(g_in[parity], 16)

            sp.wait_ge(G_ready, DT)
            load_g(0, 0)
            load_g(1, 1)
            sp.wait_ge(G_ready, DT * GROUPS)
            for parity in range(2):
                sp.wait_ge(scores_done, parity + 1)
                load_g(2 + parity, parity)
            sp.wait_ge(coef_ready, 2 * B)
            load(w2_raw.rearrange("p (t n) -> p t n", t=HT), mlp_w2, mlp_in)
            with sp.Fori(1, TILES // 2 - 1) as i:
                for parity in range(2):
                    sp.wait_ge(scores_done, i * 2 + (parity + 1))
                    load_g(i * 2 + (2 + parity), parity)

            with sp.Fori(0, B) as b:
                for t in range(0, KT, 2):
                    sp.wait_ge(rows_done, b * KT + (TILES + t + 2))
                    sp.dma_start(out_v[:, ds(b, 1), t:t + 2, :].rearrange("p b t n -> p (b t) n"),
                                 x_rows[:, ds(b * KT + t, 2), :]).then_inc(stored, 16)
            sp.wait_ge(stored, 16 * TILES // 2)

        @block.gpsimd
        def _(pool):
            pool.memset(ident[:, :], 0.0).then_inc(zeroed, 1)
            pool.memset(power[:, :], -0.5).then_inc(ones_ready, 1)
            pool.wait_ge(zeroed, 1)
            pool.affine_select(out=ident[:, :], in_=ident[:, :], compare_op=ALU.not_equal, fill=1.0,
                               base=0, pattern=[[-1, P]], channel_multiplier=1).then_inc(ident_ready, 1)
            pool.wait_ge(ones_ready, 1)

            def inverse_rms(n):
                cols = ds(n * GT, GT)
                pool.wait_ge(sq_done, n + 1)
                if n < 2:
                    pool.wait_ge(dve_sq_done, n + 1)
                pool.tensor_scalar(meansq[:, cols], sumsq[:, cols], 1.0 / D, EPS, ALU.mult, ALU.add
                                   ).then_inc(mean_done, 1)
                pool.wait_ge(mean_done, n + 1)
                pool.tensor_tensor(rstd[:, cols], meansq[:, cols], power[:, :], ALU.pow).then_inc(rstd_done, 1)

            def high_columns(n, g):
                for d in range(DT):
                    pool.wait_ge(h_done, n * DT + d + 1)
                    pool.tensor_scalar(hT[:, HI, d, g * GW:(g + 1) * GW], h_full[:, d, :], 1.0, 0.0, ALU.mult, ALU.add
                                       ).then_inc(h_hi, 1)

            def normed_rows(n, tiles):
                pool.wait_ge(rstd_done, n + 1)
                for j in tiles:
                    t = n * GT + j
                    pool.tensor_scalar(xn[:, j, :], x_rows[:, t, :], rstd[:, t:t + 1], 0.0, ALU.mult, ALU.add
                                       ).then_inc(xn_done, 1)

            inverse_rms(0)
            normed_rows(0, range(GT // 2, GT))
            pool.wait_ge(vec_in, 16)
            pool.wait_ge(ident_ready, 1)
            for d in range(DT):
                pool.tensor_scalar(bv_wide[:, d, :], ident[:, :], 0.0, vcol[:, VB + d:VB + d + 1], ALU.mult, ALU.add
                                   ).then_inc(wide_ready, 1)
            for g in range(1, GROUPS):
                if g > 1:
                    inverse_rms(g)
                high_columns(g - 1, g - 1)
                if g == 1:
                    inverse_rms(g)
                pool.wait_ge(xT_done, g)
                normed_rows(g, range(GT if g > 1 else GT - 1))
            high_columns(GROUPS - 1, GROUPS - 1)

            pool.wait_ge(addrow_ready, 1)
            pool.wait_ge(xn_done, TILES)
            with pool.Fori(0, TILES) as t:
                row = x_rows[:, ds(t, 1), :].rearrange("p t n -> p (t n)")
                pool.tensor_tensor(row, row, add_row[:, 0, :], ALU.add).then_inc(residual_ready, 1)

            pool.wait_ge(mlp_in, 32)
            for src, dst in ((w1_raw, w1_flat), (w2_raw, w2_flat)):
                for c in range(0, 2048, 512):
                    s = slice(c, c + 512)
                    pool.tensor_scalar(dst[:, HI, s], src[:, s], 1.0, 0.0, ALU.mult, ALU.add).then_inc(mlp_hi, 1)
            for n, (src, dst) in enumerate(((w1_raw, w1_flat), (w2_raw, w2_flat))):
                pool.wait_ge(mlp_hi, 4 * (n + 1))
                for c in range(0, 2048, 512):
                    s = slice(c, c + 512)
                    pool.tensor_tensor(dst[:, LO, s], src[:, s], dst[:, HI, s].bitcast(F32), ALU.subtract
                                       ).then_inc(mlp_ready, 1)

            for g in range(GROUPS):
                inverse_rms(g + GROUPS)
                pool.wait_ge(xn_done, TILES + GT * (g + 1))
                for j in range(GT):
                    row = x_rows[:, ds(g * GT + j, 1), :].rearrange("p t n -> p (t n)")
                    pool.tensor_tensor(row, row, add_row[:, 1, :], ALU.add).then_inc(residual_ready, 1)
                high_columns(g + GROUPS, g)

        @block.scalar
        def _(act):
            def squares(g, tiles=GT):
                act.wait_ge(x_in[g] if g > 0 else x_half_in, 16)
                for j in range(tiles):
                    t = g * GT + j
                    last = act.activation(V_all[:, t, 0, :], x_rows[:, t, :], ACT.Square,
                                          accum_out=sumsq[:, t:t + 1])
                last.then_inc(sq_done, 1)

            def columns(n, which, b):
                act.wait_ge(xT_done, n + 1)
                for d in range(DT):
                    act.activation(h_full[:, d, :], bank(d), ACT.Identity, bias=coef[:, which, b, DT + d],
                                   scale=coef[:, which, b, d]).then_inc(h_done, 1)

            def high_G(g):
                for d in range(DT):
                    act.wait_ge(G_done, DT * g + d + 1)
                    act.activation(G_all[:, g * GT:(g + 1) * GT, HI, d, :],
                                   bank(2 + d).rearrange("p (t n) -> p t n", t=GT), ACT.Identity,
                                   bias=small[:, d:d + 1]).then_inc(G_hi, 1)

            def high_V(g):
                for j in range(GT):
                    act.wait_ge(V_done, GT * g + j + 1)
                    act.copy(V_all[:, g * GT + j, HI, :], bank(4 + j, D)).then_inc(V_hi, 1)

            squares(0, GT // 2)
            for i in range(DT):
                act.wait_ge(qk_done, i + 1)
                act.copy(qk_w[:, HI, i, :], bank(4 + i, D)).then_inc(qk_hi, 1)
                act.copy(vp_w[:, HI, i, D:VW], bank(4 + i)[:, D:VW]).then_inc(qk_hi, 1)
            act.wait_ge(coef_ready, 1)
            columns(0, 0, slice(0, 1))
            squares(1, GT // 2)
            act.wait_ge(vp_done, 1)
            act.copy(vp_w[:, HI, :, 0:D], bank(6).rearrange("p (t n) -> p t n", t=DT)).then_inc(vp_hi, 1)
            squares(2)
            act.wait_ge(bias_ready, DT + 1)
            high_G(0)
            for g in range(1, GROUPS):
                act.wait_ge(h_ready, DT * g)
                act.wait_ge(coef_ready, g // 2 + 1)
                columns(g, 0, slice(g // 2, g // 2 + 1))
                high_V(g - 1)
                if g == 1:
                    squares(3)
                high_G(g)
            high_V(GROUPS - 1)

            def exp(t, parity):
                act.wait_ge(exp_bias_ready, t + 1)
                act.activation(probs[:, parity, :], psum[:, 2 * parity:2 * parity + 2, :].rearrange("p a n -> p (a n)"),
                               ACT.Exp, bias=exp_bias[:, ds(t, 1)], scale=SCALE,
                               accum_out=row_sum[:, ds(t, 1)]).then_inc(exp_done, 1)

            def turned_hi(t, parity):
                for half in range(2):
                    act.wait_ge(probs_turned, t * 2 + (half + 1))
                    act.copy(probsT[:, parity, HI, 4 * half:4 * half + 4, :].rearrange("p k n -> p (k n)"),
                             bank(4 + half)).then_inc(probsT_hi, 1)

            def tile(t, parity):
                exp(t + 1, 1 - parity)
                turned_hi(t, parity)

            def tile_pair(i):
                for k in (1, 2):
                    tile(i * 2 + k, k % 2)

            def squares_after(g, tiles=range(GT)):
                act.wait_ge(rows_done, g * GT + GT)
                act.wait_ge(xT_done, g + GROUPS)
                for j in tiles:
                    last = act.activation(xn[:, j, :], x_rows[:, ds(g * GT + j, 1), :].rearrange("p t n -> p (t n)"),
                                          ACT.Square, accum_out=sumsq[:, ds(g * GT + (TILES + j), 1)])
                if GT - 1 in tiles:
                    last.then_inc(sq_done, 1)

            def columns_after(g):
                act.wait_ge(h_ready, g * DT + DT * GROUPS)
                columns(g + GROUPS, 1, ds(g // 2, 1))

            exp(0, 0)
            turned_hi(0, 0)
            exp(1, 1)
            with act.Fori(0, LAST - 2) as i:
                tile_pair(i)
            for half in range(2):
                squares_after(0, range(half * GT // 2, (half + 1) * GT // 2))
                tile_pair(LAST - 2 + half)
            tile(TILES - 3, 1)
            turned_hi(TILES - 2, 0)
            exp(TILES - 1, 1)
            columns_after(0)
            turned_hi(TILES - 1, 1)

            def gelu_tile(g, m, before):
                n = g * HT + m
                act.wait_ge(hidden_done, n + 1)
                if before or m >= 2:
                    act.wait_ge(gelu_ready, n - 1)
                for dst in (gelu_full[:, m % 2, :], gelu[:, m, HI, :]):
                    act.activation(dst, bank(2 + m % 2), ACT.Gelu, bias=vcol[:, B1 + m:B1 + m + 1]
                                   ).then_inc(gelu_done, 1)

            def mlp(g, before, more):
                for m in range(HT):
                    gelu_tile(g, m, before)
                    if more and m == 0:
                        squares_after(g + 1)
                    if more and m == 5:
                        columns_after(g + 1)

            mlp(0, False, True)
            with act.Fori(1, GROUPS - 1) as g:
                mlp(g, True, True)
            mlp(GROUPS - 1, True, False)

        @block.vector
        def _(dve):
            def film_products(f, b, place):
                for k in range(2 * DT):
                    dve.tensor_tensor_reduce(place(b * 2 * DT + k), film_wT[f][:, k, :], wide_rows[:, b, :], 1.0, 0.0,
                                             ALU.mult, ALU.add, film_sum[:, f, b, k:k + 1]).then_inc(film_sums, 1)

            def coefficients(f, b):
                n = f * B + b + 1
                dve.wait_ge(film_sums, 2 * DT * n)
                if n == 1:
                    dve.wait_ge(vec_in, 16)
                dve.tensor_tensor(coef[:, f, b, :], film_sum[:, f, b, :], vcol[:, FB[f]:FB[f] + 2 * DT], ALU.add
                                  ).then_inc(shift_ready, 1)
                dve.wait_ge(shift_ready, n)
                dve.scalar_tensor_tensor(out=coef[:, f, b, 0:DT], in0=coef[:, f, b, 0:DT], scalar=1.0,
                                         in1=vcol[:, NORM[f]:NORM[f] + DT], op0=ALU.add, op1=ALU.mult
                                         ).then_inc(coef_ready, 1)

            def normed_rows(n, t, tiles=range(GT)):
                dve.wait_ge(rstd_done, n + 1)
                for j in tiles:
                    dve.tensor_scalar(xn[:, j, :], x_rows[:, ds(t + j, 1), :].rearrange("p t n -> p (t n)"),
                                      rstd[:, ds(n * GT + j, 1)], None, ALU.mult).then_inc(xn_done, 1)

            def squares(g):
                dve.wait_ge(x_in[g], 16)
                for t in range(g * GT + GT // 2, (g + 1) * GT):
                    last = dve.tensor_tensor_reduce(V_all[:, t, 0, :], x_rows[:, t, :], x_rows[:, t, :], 1.0, 0.0,
                                                    ALU.mult, ALU.add, sumsq[:, t:t + 1])
                last.then_inc(dve_sq_done, 1)

            def low_columns(n, tokens):
                for d in range(DT):
                    dve.wait_ge(h_hi, n * DT + (d + 1))
                    dve.tensor_tensor(hT[:, LO, d, tokens], h_full[:, d, :], hT[:, HI, d, tokens].bitcast(F32),
                                      ALU.subtract).then_inc(h_ready, 1)

            def g_place(part):
                return lambda n: G_all[:, n, part, :, :].rearrange("p t n -> p (t n)")

            squares(0)
            normed_rows(0, 0, range(GT // 2))
            dve.wait_ge(wide_in, 16)
            dve.wait_ge(film_in[0], 16)
            film_products(0, 0, g_place(LO))
            coefficients(0, 0)
            for i in range(DT):
                dve.wait_ge(qk_hi, 2 * i + 2)
                dve.tensor_tensor(qk_w[:, LO, i, :], bank(4 + i, D), qk_w[:, HI, i, :].bitcast(F32), ALU.subtract
                                  ).then_inc(qk_ready, 1)
                dve.tensor_tensor(vp_w[:, LO, i, D:VW], bank(4 + i)[:, D:VW], vp_w[:, HI, i, D:VW].bitcast(F32),
                                  ALU.subtract).then_inc(qk_ready, 1)
            squares(1)
            low_columns(0, slice(0, GW))
            dve.wait_ge(k_in, 32)
            bq, bk = wide_rows[:, B, :], wide_rows[:, B + 1, :]
            for n, (a, b) in enumerate([(wk[:, j, :], bq) for j in range(DT)] + [(bk, bq)]):
                dve.tensor_tensor_reduce(g_place(HI)(n), a, b, 1.0, 0.0,
                                         ALU.mult, ALU.add, small[:, n:n + 1]).then_inc(bias_ready, 1)
            dve.wait_ge(vp_hi, 1)
            dve.tensor_tensor(vp_w[:, LO, :, 0:D], bank(6).rearrange("p (t n) -> p t n", t=DT),
                              vp_w[:, HI, :, 0:D].bitcast(F32), ALU.subtract).then_inc(vp_ready, 1)
            dve.wait_ge(xT_done, 1)
            normed_rows(1, GT, range(GT - 1, GT))
            dve.wait_ge(addrow_done, 1)
            dve.wait_ge(rows_in, 16)
            dve.tensor_tensor(add_row[:, 0, :], bank(7, D), add_row[:, 0, :], ALU.add).then_inc(addrow_ready, 1)
            dve.wait_ge(bias_ready, DT + 1)

            def low_G(g):
                for d in range(DT):
                    dve.wait_ge(G_hi, DT * g + d + 1)
                    dve.scalar_tensor_tensor(out=G_all[:, g * GT:(g + 1) * GT, LO, d, :],
                                             in0=bank(2 + d).rearrange("p (t n) -> p t n", t=GT),
                                             scalar=small[:, d:d + 1],
                                             in1=G_all[:, g * GT:(g + 1) * GT, HI, d, :].bitcast(F32),
                                             op0=ALU.add, op1=ALU.subtract).then_inc(G_ready, 1)

            def low_V(g):
                for j in range(GT):
                    t = g * GT + j
                    dve.wait_ge(V_hi, t + 1)
                    dve.tensor_scalar(key_term[:, t:t + 1], bank(4 + j)[:, D:D + 1], small[:, 2:3], None, ALU.add)
                    dve.tensor_tensor(V_all[:, t, LO, :], bank(4 + j, D), V_all[:, t, HI, :].bitcast(F32),
                                      ALU.subtract).then_inc(V_ready, 1)

            def late_place(n):
                return V_all[:, TILES - GT + n % GT, LO, :]

            film_products(0, 1, late_place)
            coefficients(0, 1)
            low_G(0)
            for g in range(1, GROUPS):
                low_columns(g, slice(g * GW, (g + 1) * GW))
                low_V(g - 1)
                low_G(g)
                if g > 1:
                    dve.wait_ge(film_in[1], 16)
                    film_products(1, g - 2, late_place)
                    coefficients(1, g - 2)

            def row_maximum(t, parity):
                col = ds(t, 1)
                dve.wait_ge(scores_done, t + 1)
                dve.reduce_max(row_max[:, col], psum[:, 2 * parity:2 * parity + 2, :].rearrange("p a n -> p (a n)"),
                               AX_X).then_inc(max_done, 1)
                dve.wait_ge(max_done, t + 1)
                dve.tensor_tensor(true_max[:, col], row_max[:, col], key_term[:, col], ALU.add
                                  ).then_inc(true_max_done, 1)
                dve.wait_ge(true_max_done, t + 1)
                dve.tensor_scalar(exp_bias[:, col], true_max[:, col], key_term[:, col], -SCALE,
                                  ALU.subtract, ALU.mult).then_inc(exp_bias_ready, 1)

            def turned_lo(t, parity):
                for half in range(2):
                    dve.wait_ge(probsT_hi, t * 2 + (half + 1))
                    k = slice(4 * half, 4 * half + 4)
                    dve.tensor_tensor(probsT[:, parity, LO, k, :].rearrange("p k n -> p (k n)"), bank(4 + half),
                                      probsT[:, parity, HI, k, :].rearrange("p k n -> p (k n)").bitcast(F32),
                                      ALU.subtract).then_inc(probsT_ready, 1)

            def add_attention(t, parity):
                col = ds(t, 1)
                dve.wait_ge(attn_done, t + 1)
                dve.reciprocal(row_inv[:, col], row_sum[:, col]).then_inc(inv_done, 1)
                dve.wait_ge(inv_done, t + 1)
                dve.wait_ge(residual_ready, t + 1)
                row = x_rows[:, col, :].rearrange("p t n -> p (t n)")
                dve.scalar_tensor_tensor(out=row, in0=bank(6 + parity, D), scalar=row_inv[:, col], in1=row,
                                         op0=ALU.mult, op1=ALU.add).then_inc(rows_done, 1)

            def tile(t, parity):
                turned_lo(t - 1, 1 - parity)
                row_maximum(t + 1, 1 - parity)
                add_attention(t - 1, 1 - parity)

            def tile_pair(i):
                for k in (1, 2):
                    tile(i * 2 + k, k % 2)

            row_maximum(0, 0)
            low_V(GROUPS - 1)
            row_maximum(1, 1)
            with dve.Fori(0, LAST) as i:
                tile_pair(i)
            normed_rows(GROUPS, 0)
            tile(TILES - 3, 1)
            turned_lo(TILES - 3, 1)
            row_maximum(TILES - 1, 1)
            turned_lo(TILES - 2, 0)
            add_attention(TILES - 3, 1)
            low_columns(GROUPS, slice(0, GW))
            add_attention(TILES - 2, 0)
            turned_lo(TILES - 1, 1)

            def gelu_low(g, m):
                n = g * HT + m
                dve.wait_ge(gelu_done, n * 2 + 2)
                dve.tensor_tensor(gelu[:, m, LO, :], gelu_full[:, m % 2, :], gelu[:, m, HI, :].bitcast(F32),
                                  ALU.subtract).then_inc(gelu_ready, 1)

            def finished_rows(g):
                for j in range(GT):
                    dve.wait_ge(mlp_done, g * GT + (j + 1))
                    dve.wait_ge(residual_ready, g * GT + (TILES + j + 1))
                    row = x_rows[:, ds(g * GT + j, 1), :].rearrange("p t n -> p (t n)")
                    dve.tensor_tensor(row, bank(4 + j, D), row, ALU.add).then_inc(rows_done, 1)

            def mlp(g, before, more):
                for m in range(HT):
                    gelu_low(g, m)
                    if not before and m == 0:
                        add_attention(TILES - 1, 1)
                    if before and m == 0:
                        finished_rows(g - 1)
                    if more and m == 2:
                        normed_rows(g + (GROUPS + 1), g * GT + GT)
                    if more and m == 6:
                        low_columns(g + (GROUPS + 1), ds(g * GW + GW, GW))

            mlp(0, False, True)
            with dve.Fori(1, GROUPS - 1) as g:
                mlp(g, True, True)
            mlp(GROUPS - 1, True, False)
            finished_rows(GROUPS - 1)

        @block.tensor
        def _(pe):
            def transpose_rows(n):
                pe.wait_ge(xn_done, n * GT + GT)
                for d in range(DT):
                    for j in range(GT):
                        last = pe.transpose(bank(d)[:, j * P:(j + 1) * P], xn[:, j, d * P:(d + 1) * P], ident[:, :])
                last.then_inc(xT_done, 1)

            def split_matmul(dst, stationary, moving, tiles):
                n = len(tiles) * len(PASSES)
                for a, b in PASSES:
                    for k in tiles:
                        n -= 1
                        last = pe.matmul(dst, stationary(a, k), moving(b, k),
                                         start=(n == len(tiles) * len(PASSES) - 1), stop=(n == 0))
                return last

            def project_g(g):
                if g > 0:
                    pe.wait_ge(G_ready, DT * g)
                s = slice(g * GW, (g + 1) * GW)
                pe.wait_ge(h_hi, DT * (g + 1))
                for j in range(DT):
                    for k in range(DT):
                        pe.matmul(bank(2 + j), qk_w[:, LO, k, j * P:(j + 1) * P], hT[:, HI, k, s],
                                  start=(k == 0), stop=False)
                pe.wait_ge(h_ready, DT * (g + 1))
                for j in range(DT):
                    for part in (LO, HI):
                        for k in range(DT):
                            last = pe.matmul(bank(2 + j), qk_w[:, HI, k, j * P:(j + 1) * P], hT[:, part, k, s],
                                             start=False, stop=(part == HI and k == DT - 1))
                    last.then_inc(G_done, 1)

            def project_v(g):
                for j in range(GT):
                    if g > 0:
                        pe.wait_ge(V_ready, GT * (g - 1) + j + 1)
                    t = g * GT + j
                    split_matmul(bank(4 + j, VW), lambda a, k: hT[:, a, k, t * P:(t + 1) * P],
                                 lambda b, k: vp_w[:, b, k, :], range(DT)).then_inc(V_done, 1)

            for e in range(DT):
                pe.wait_ge(wqk_in[e], 16)
                for i in range(DT):
                    last = pe.matmul(bank(4 + i, KW), wqT[:, e, i * P:(i + 1) * P], wkT[:, e, :],
                                     start=(e == 0), stop=(e == DT - 1))
                    if e == DT - 1:
                        last.then_inc(qk_done, 1)
            pe.wait_ge(ident_ready, 1)
            transpose_rows(0)
            pe.wait_ge(wvp_in, 16)
            for i in range(DT):
                for e in range(DT):
                    last = pe.matmul(bank(6)[:, i * D:(i + 1) * D], wvT[:, e, i * P:(i + 1) * P], wp[:, e, :],
                                     start=(e == 0), stop=(e == DT - 1))
            last.then_inc(vp_done, 1)
            pe.wait_ge(wide_ready, DT)
            for e in range(DT):
                last = pe.matmul(bank(7, D), bv_wide[:, e, :], wp[:, e, :], start=(e == 0), stop=(e == DT - 1))
            last.then_inc(addrow_done, 1)

            def scores(t, parity, b):
                for half in range(2):
                    last = split_matmul(bank(2 * parity + half), lambda a, k: g_tile[:, parity, a, k, :],
                                        lambda s, k: hT[:, s, k, ds(b * N + half * 512, 512)], range(DT))
                last.then_inc(scores_done, 1)

            def transpose_probs(t, parity):
                pe.wait_ge(exp_done, t + 1)
                for half in range(2):
                    for j in range(4):
                        k = 4 * half + j
                        last = pe.transpose(bank(4 + half)[:, j * P:(j + 1) * P], probs[:, parity, k * P:(k + 1) * P],
                                            ident[:, :])
                    last.then_inc(probs_turned, 1)

            def attention(t, parity, b):
                n = 0
                for half in range(2):
                    pe.wait_ge(probsT_ready, t * 2 + (half + 1))
                    for k in range(4 * half, 4 * half + 4):
                        for a, s in PASSES:
                            last = pe.matmul(bank(6 + parity, D), probsT[:, parity, a, k, :],
                                             V_all[:, ds(b * KT + k, 1), s, :].rearrange("p t n -> p (t n)"),
                                             start=(n == 0), stop=(n == KT * len(PASSES) - 1))
                            n += 1
                last.then_inc(attn_done, 1)

            pe.wait_ge(qk_ready, 2 * DT)
            for g in range(GROUPS):
                project_g(g)
                if g + 1 < GROUPS:
                    pe.wait_ge(h_done, DT * (g + 1))
                    transpose_rows(g + 1)
                else:
                    pe.wait_ge(h_done, DT * GROUPS)
                    pe.wait_ge(g_in[0], 16)
                    scores(0, 0, 0)
                if g == 0:
                    pe.wait_ge(vp_ready, 1)
                    pe.wait_ge(addrow_ready, 1)
                project_v(g)

            pe.wait_ge(G_ready, DT * GROUPS)
            pe.wait_ge(g_in[1], 16)
            scores(1, 1, 0)
            pe.wait_ge(V_ready, TILES)
            transpose_probs(0, 0)
            with pe.Fori(0, LAST) as i:
                for k in (1, 2):
                    nxt, now = (k + 1) % 2, k % 2
                    pe.wait_ge(g_in[nxt], (i * 2 + (k + 1)) // 2 * 16 + 16)
                    scores(None, nxt, (i * 2 + (k + 1)) // KT)
                    attention(i * 2 + (k - 1), nxt, (i * 2 + (k - 1)) // KT)
                    transpose_probs(i * 2 + k, now)
            pe.wait_ge(g_in[0], 16 * TILES // 2)
            scores(TILES - 2, 0, B - 1)
            attention(TILES - 4, 0, B - 1)
            transpose_probs(TILES - 3, 1)
            pe.wait_ge(g_in[1], 16 * TILES // 2)
            scores(TILES - 1, 1, B - 1)
            pe.wait_ge(probsT_ready, 2 * (TILES - 2))
            transpose_probs(TILES - 2, 0)
            transpose_rows(GROUPS)
            attention(TILES - 3, 1, B - 1)
            attention(TILES - 2, 0, B - 1)
            transpose_probs(TILES - 1, 1)

            def hidden(g, m, before=True):
                n = g * HT + m
                if before:
                    pe.wait_ge(gelu_done, n * 2 - 2)
                split_matmul(bank(2 + m % 2), lambda a, k: w1[:, a, k, m * P:(m + 1) * P],
                             lambda b, k: hT[:, b, k, ds(g * GW, GW)], range(DT)).then_inc(hidden_done, 1)

            def project_hidden(g, m, before=True):
                pe.wait_ge(gelu_ready, g * HT + (m + 1))
                for j in range(GT):
                    if m == 0 and before:
                        pe.wait_ge(rows_done, g * GT + (TILES - GT + j + 1))
                    for n, (a, b) in enumerate(PASSES):
                        last = pe.matmul(bank(4 + j, D), gelu[:, m, a, j * P:(j + 1) * P], w2[:, b, m, :],
                                         start=(m == 0 and n == 0), stop=(m == HT - 1 and n == len(PASSES) - 1))
                    if m == HT - 1:
                        last.then_inc(mlp_done, 1)

            def mlp(g, before, more):
                for m in range(HT):
                    if before or m >= 2:
                        if m == 0:
                            pe.wait_ge(h_ready, g * DT + DT * (GROUPS + 1))
                        hidden(g, m)
                    if more and m == 4:
                        transpose_rows(g + (GROUPS + 1))
                    if m == 2 and not before:
                        pe.wait_ge(rows_done, TILES)
                    if m >= 2:
                        project_hidden(g, m - 2, before)
                    elif before:
                        project_hidden(g - 1, HT - 2 + m)

            pe.wait_ge(mlp_ready, 8)
            pe.wait_ge(h_ready, DT * (GROUPS + 1))
            hidden(0, 0, False)
            hidden(0, 1, False)
            attention(TILES - 1, 1, B - 1)
            mlp(0, False, True)
            with pe.Fori(1, GROUPS - 1) as g:
                mlp(g, True, True)
            mlp(GROUPS - 1, True, False)
            for m in (HT - 2, HT - 1):
                project_hidden(GROUPS - 1, m)


def laid_out(x, cond_1024, **w):
    import numpy as np

    w = {k.removeprefix("L0_cond_"): np.asarray(v) for k, v in w.items()}

    def by_partition(a):
        return np.ascontiguousarray(a.reshape(-1, P, a.shape[1]).transpose(1, 0, 2))

    def side_by_side(*arrays):
        return np.ascontiguousarray(np.concatenate([by_partition(a).reshape(P, -1) for a in arrays], axis=1))

    wk_bk = np.concatenate([w["k_w"].T, w["k_b"].reshape(-1, 1), w["k_b"].reshape(-1, 1)], axis=1)
    vectors = [w[n] for n in ("norm1_w", "film1_b", "v_b", "norm2_w", "film2_b", "mlp_b1")]
    vectors = np.concatenate([v.reshape(-1, P) for v in vectors], axis=0)
    return {
        "x": np.ascontiguousarray(x),
        "vectors": np.ascontiguousarray(vectors.T),
        "rows": np.concatenate([np.asarray(cond_1024), w["q_b"][None], w["k_b"][None]], axis=0),
        "qk_weights": by_partition(np.concatenate([w["q_w"].T, wk_bk], axis=1)),
        "vp_weights": side_by_side(w["v_w"].T, w["proj_w"]),
        "k_w": by_partition(w["k_w"]),
        "film1_wT": by_partition(w["film1_w"].T),
        "film2_wT": by_partition(w["film2_w"].T),
        "out_bias": np.stack([w["proj_b"], w["mlp_b2"]]),
        "mlp_w1": by_partition(w["mlp_w1"]),
        "mlp_w2": by_partition(w["mlp_w2"]),
    }


def kernel(**inputs):
    import concourse.bacc as _bacc
    from concourse import mybir as _mybir
    from concourse.bass_utils import run_bass_kernel_spmd as _run

    nc = _bacc.Bacc("TRN2", target_bir_lowering=False, num_devices=1)
    arrays, args = {}, []
    for name, a in laid_out(**inputs).items():
        arrays[f"in_{name}_dram"] = a
        args.append(nc.dram_tensor(f"in_{name}_dram", a.shape, _mybir.dt.from_np(a.dtype), kind="ExternalInput").ap())
    shape = arrays["in_x_dram"].shape
    args.append(nc.dram_tensor("out_0_dram", shape, _mybir.dt.float32, kind="ExternalOutput").ap())
    film_block_kernel(nc, *args)
    r = _run(nc, [arrays], core_ids=[0])
    return r.results[0]["out_0_dram"]
```
